# Optimizing a Trainium2 kernel written in Bass

```python
import numpy as np
import jax
import jax.numpy as jnp

def _softmax(x, axis=-1):
    return jax.nn.softmax(x, axis=axis)

def _gelu(x):
    return jax.nn.gelu(x, approximate=True)

def _silu(x):
    return jax.nn.silu(x)

def _sigmoid(x):
    return jax.nn.sigmoid(x)

def _layernorm(x, axis=-1, eps=1e-05):
    m = jnp.mean(x, axis=axis, keepdims=True)
    v = jnp.var(x, axis=axis, keepdims=True)
    return (x - m) / jnp.sqrt(v + eps)

def _scatter_add(tgt, idx, src, axis=0):
    return tgt.at[idx].add(src)

def _segment_sum(src, seg, n):
    return jax.ops.segment_sum(src, seg, n)
kernel_name = 'mk_gnn_resnorm_d4_gnn_r8_d8fac7'

def setup_inputs(seed: int=0):
    np.random.seed(seed)
    _w = jnp.asarray

    def _rec_inputs():
        import jax
        import jax.numpy as jnp
        _gk = jax.random.key(seed)
        x = 0.0001712 + 1 * jax.random.normal(jax.random.fold_in(_gk, 1), (12500, 16), jnp.float32)
        src = jax.random.randint(jax.random.fold_in(_gk, 2), (400000,), 0, 12500, jnp.int32)
        dst = jnp.minimum((12500 * jax.random.uniform(jax.random.fold_in(_gk, 3), (400000,)) ** 2.0).astype(jnp.int32), 99999)
        _o = jnp.argsort(dst, stable=True)
        src = src[_o]
        dst = dst[_o]
        edge_attr_3 = -1.09012e-05 + 0.99985 * jax.random.normal(jax.random.fold_in(_gk, 11), (400000, 3), jnp.float32)
        edge_attr_48 = -3.69585e-06 + 0.999911 * jax.random.normal(jax.random.fold_in(_gk, 12), (400000, 48), jnp.float32)
        edge_attr_8 = 0.000714719 + 1.00021 * jax.random.normal(jax.random.fold_in(_gk, 13), (400000, 8), jnp.float32)
        return (x, src, dst, edge_attr_3, edge_attr_48, edge_attr_8)
    x, src, dst, edge_attr_3, edge_attr_48, edge_attr_8 = _rec_inputs()

    def _L0_gnn_setup():
        import jax, jax.numpy as jnp
        import numpy as np
        STALK_DIM = 16
        N_NODES = 6250
        N_EDGES = 50000
        HIDDEN = 64
        key = jax.random.key(seed)
        k1, k2, k3, k4 = jax.random.split(key, 4)
        d = STALK_DIM
        x = jax.random.normal(k1, (N_NODES, d), dtype=jnp.float32)
        edge_index = jax.random.randint(k2, (2, N_EDGES), 0, N_NODES, dtype=jnp.int64)
        W1 = jax.random.normal(k3, (HIDDEN, 2 * d), dtype=jnp.float32) * (1.0 / np.sqrt(2 * d))
        b1 = jnp.zeros((HIDDEN,), dtype=jnp.float32)
        W2 = jax.random.normal(k4, (d, HIDDEN), dtype=jnp.float32) * (1.0 / np.sqrt(HIDDEN))
        b2 = jnp.zeros((d,), dtype=jnp.float32)
        return {'x': x, 'edge_index': edge_index, 'W1': W1, 'b1': b1, 'W2': W2, 'b2': b2}
    _L0_gnn_all = _L0_gnn_setup()
    _L0_gnn_in = {k: v for k, v in _L0_gnn_all.items() if k in ('W1', 'b1', 'W2', 'b2')}
    del _L0_gnn_all

    def _L1_gnn_setup():
        import jax, jax.numpy as jnp
        import numpy as np
        NS, NV = (16, 4)
        EPS = 1e-05
        N_NODES, N_EDGES = (5000, 50000)

        def _bn_scalar(x, g, b):
            m = x.mean(0)
            v = ((x - m) ** 2).mean(0)
            return (x - m) / jnp.sqrt(v + EPS) * g + b

        def _seg_mean(x, idx, n):
            s = jax.ops.segment_sum(x, idx, num_segments=n)
            c = jax.ops.segment_sum(jnp.ones((idx.shape[0],), x.dtype), idx, num_segments=n)
            return s / jnp.maximum(c, 1.0)[:, None]

        def _edge_weights(edge_attr, w1, b1, w2, b2):
            h = jax.nn.relu(edge_attr @ w1 + b1)
            return h @ w2 + b2

        def _forward(node_attr, edge_attr, edge_vec, fc0_w1, fc0_b1, fc0_w2, fc0_b2, fc1_w1, fc1_b1, fc1_w2, fc1_b2, bn0_gs, bn0_bs, bn0_gv, bn1_gs, bn1_bs, edge_index):
            N = node_attr.shape[0]
            E = edge_attr.shape[0]
            src, dst = (edge_index[0], edge_index[1])
            rhat = edge_vec / (jnp.linalg.norm(edge_vec, axis=-1, keepdims=True) + 1e-12)
            sh1 = rhat * float(np.sqrt(3.0))
            w = _edge_weights(edge_attr, fc0_w1, fc0_b1, fc0_w2, fc0_b2)
            wa = w[:, :NS * NS].reshape(E, NS, NS)
            wb = w[:, NS * NS:].reshape(E, NS, NV)
            x = node_attr[dst]
            inv = float(1.0 / np.sqrt(NS))
            msg_s = jnp.einsum('ei,eij->ej', x, wa) * inv
            msg_v = jnp.einsum('ei,eij,ec->ejc', x, wb, sh1) * inv
            msg = jnp.concatenate([msg_s, msg_v.reshape(E, NV * 3)], axis=-1)
            out = _seg_mean(msg, src, N)
            s0 = _bn_scalar(out[:, :NS], bn0_gs, bn0_bs)
            v0 = out[:, NS:].reshape(N, NV, 3)
            vn = jnp.sqrt((v0 ** 2).mean(axis=(0, 2)) + EPS)
            v0 = v0 / vn[None, :, None] * bn0_gv[None, :, None]
            w = _edge_weights(edge_attr, fc1_w1, fc1_b1, fc1_w2, fc1_b2)
            wa = w[:, :NS * NS].reshape(E, NS, NS)
            wb = w[:, NS * NS:].reshape(E, NV, NS)
            s = s0[dst]
            v = v0[dst]
            path_a = jnp.einsum('ei,eij->ej', s, wa)
            path_b = jnp.einsum('eic,ec,eij->ej', v, sh1, wb) * float(1.0 / np.sqrt(3.0))
            msg = (path_a + path_b) * float(1.0 / np.sqrt(NS + NV))
            node1 = _seg_mean(msg, src, N)
            return _bn_scalar(node1, bn1_gs, bn1_bs)
        key = jax.random.key(seed)
        ks = jax.random.split(key, 8)
        d = 3 * NS
        wn = NS * NS + NS * NV
        g = lambda k, shape, sc: jax.random.normal(k, shape, jnp.float32) * sc
        return {'node_attr': g(ks[0], (N_NODES, NS), 1.0), 'edge_attr': g(ks[1], (N_EDGES, d), 1.0), 'edge_vec': g(ks[2], (N_EDGES, 3), 1.0), 'fc0_w1': g(ks[3], (d, d), d ** (-0.5)), 'fc0_b1': jnp.zeros((d,), jnp.float32), 'fc0_w2': g(ks[4], (d, wn), d ** (-0.5)), 'fc0_b2': jnp.zeros((wn,), jnp.float32), 'fc1_w1': g(ks[5], (d, d), d ** (-0.5)), 'fc1_b1': jnp.zeros((d,), jnp.float32), 'fc1_w2': g(ks[6], (d, wn), d ** (-0.5)), 'fc1_b2': jnp.zeros((wn,), jnp.float32), 'bn0_gs': jnp.ones((NS,), jnp.float32), 'bn0_bs': jnp.zeros((NS,), jnp.float32), 'bn0_gv': jnp.ones((NV,), jnp.float32), 'bn1_gs': jnp.ones((NS,), jnp.float32), 'bn1_bs': jnp.zeros((NS,), jnp.float32), 'edge_index': jax.random.randint(ks[7], (2, N_EDGES), 0, N_NODES)}
    _L1_gnn_all = _L1_gnn_setup()
    _L1_gnn_in = {k: v for k, v in _L1_gnn_all.items() if k in ('fc0_w1', 'fc0_b1', 'fc0_w2', 'fc0_b2', 'fc1_w1', 'fc1_b1', 'fc1_w2', 'fc1_b2', 'bn0_gs', 'bn0_bs', 'bn0_gv', 'bn1_gs', 'bn1_bs')}
    del _L1_gnn_all

    def _L2_gnn_setup():
        import jax, jax.numpy as jnp
        import numpy as np
        N_NODES = 6250
        N_EDGES = 50000
        D = 16
        E_FEAT = 8
        N_LAYERS = 3
        BN_EPS = 1e-05

        def _nnconv(x, src, dst, edge_attr, ew, eb, rw, rb):
            W = (edge_attr @ ew + eb).reshape(edge_attr.shape[0], x.shape[1], rw.shape[1])
            xj = x[src]
            msg = jnp.einsum('ei,eio->eo', xj, W)
            agg = jax.ops.segment_sum(msg, dst, num_segments=x.shape[0])
            return agg + x @ rw + rb

        def _batchnorm(x, gamma, beta):
            mean = jnp.mean(x, axis=0)
            var = jnp.mean(jnp.square(x - mean), axis=0)
            return (x - mean) * jax.lax.rsqrt(var + BN_EPS) * gamma + beta
        key = jax.random.key(seed)
        ks = jax.random.split(key, 12)
        x = jax.random.normal(ks[0], (N_NODES, D), dtype=jnp.float32)
        edge_index = jax.random.randint(ks[1], (2, N_EDGES), 0, N_NODES, dtype=jnp.int64)
        edge_attr = jax.random.normal(ks[2], (N_EDGES, E_FEAT), dtype=jnp.float32)
        s = 0.1
        edge_w = jax.random.normal(ks[3], (N_LAYERS, E_FEAT, D * D), dtype=jnp.float32) * s
        edge_b = jax.random.normal(ks[4], (N_LAYERS, D * D), dtype=jnp.float32) * s
        root_w = jax.random.normal(ks[5], (N_LAYERS, D, D), dtype=jnp.float32) * s
        root_b = jax.random.normal(ks[6], (N_LAYERS, D), dtype=jnp.float32) * s
        bn_gamma = jnp.ones((N_LAYERS - 1, D), dtype=jnp.float32)
        bn_beta = jnp.zeros((N_LAYERS - 1, D), dtype=jnp.float32)
        pred_w = jax.random.normal(ks[7], (D, D), dtype=jnp.float32) * s
        pred_b = jax.random.normal(ks[8], (D,), dtype=jnp.float32) * s
        return {'x': x, 'edge_index': edge_index, 'edge_attr': edge_attr, 'edge_w': edge_w, 'edge_b': edge_b, 'root_w': root_w, 'root_b': root_b, 'bn_gamma': bn_gamma, 'bn_beta': bn_beta, 'pred_w': pred_w, 'pred_b': pred_b}
    _L2_gnn_all = _L2_gnn_setup()
    _L2_gnn_in = {k: v for k, v in _L2_gnn_all.items() if k in ('edge_w', 'edge_b', 'root_w', 'root_b', 'bn_gamma', 'bn_beta', 'pred_w', 'pred_b')}
    del _L2_gnn_all

    def _L3_gnn_setup():
        import jax, jax.numpy as jnp
        import numpy as np
        N_NODES = 125000
        key = jax.random.key(seed)
        k1, k2, k3 = jax.random.split(key, 3)
        x = jax.random.normal(k1, (N_NODES, 16), dtype=jnp.float32)
        edge_index = jax.random.randint(k2, (2, 500000), 0, N_NODES, dtype=jnp.int64)
        W = jax.random.normal(k3, (16, 16), dtype=jnp.float32) * (1.0 / np.sqrt(16.0))
        b = jnp.zeros((16,), dtype=jnp.float32)
        return {'x': x, 'edge_index': edge_index, 'W': W, 'b': b}
    _L3_gnn_all = _L3_gnn_setup()
    _L3_gnn_in = {k: v for k, v in _L3_gnn_all.items() if k in ('W', 'b')}
    del _L3_gnn_all
    return {'x': x, 'src': src, 'dst': dst, 'edge_attr_3': edge_attr_3, 'edge_attr_48': edge_attr_48, 'edge_attr_8': edge_attr_8, 'L0_gnn_W1': _L0_gnn_in['W1'], 'L0_gnn_b1': _L0_gnn_in['b1'], 'L0_gnn_W2': _L0_gnn_in['W2'], 'L0_gnn_b2': _L0_gnn_in['b2'], 'L1_gnn_fc0_w1': _L1_gnn_in['fc0_w1'], 'L1_gnn_fc0_b1': _L1_gnn_in['fc0_b1'], 'L1_gnn_fc0_w2': _L1_gnn_in['fc0_w2'], 'L1_gnn_fc0_b2': _L1_gnn_in['fc0_b2'], 'L1_gnn_fc1_w1': _L1_gnn_in['fc1_w1'], 'L1_gnn_fc1_b1': _L1_gnn_in['fc1_b1'], 'L1_gnn_fc1_w2': _L1_gnn_in['fc1_w2'], 'L1_gnn_fc1_b2': _L1_gnn_in['fc1_b2'], 'L1_gnn_bn0_gs': _L1_gnn_in['bn0_gs'], 'L1_gnn_bn0_bs': _L1_gnn_in['bn0_bs'], 'L1_gnn_bn0_gv': _L1_gnn_in['bn0_gv'], 'L1_gnn_bn1_gs': _L1_gnn_in['bn1_gs'], 'L1_gnn_bn1_bs': _L1_gnn_in['bn1_bs'], 'L2_gnn_edge_w': _L2_gnn_in['edge_w'], 'L2_gnn_edge_b': _L2_gnn_in['edge_b'], 'L2_gnn_root_w': _L2_gnn_in['root_w'], 'L2_gnn_root_b': _L2_gnn_in['root_b'], 'L2_gnn_bn_gamma': _L2_gnn_in['bn_gamma'], 'L2_gnn_bn_beta': _L2_gnn_in['bn_beta'], 'L2_gnn_pred_w': _L2_gnn_in['pred_w'], 'L2_gnn_pred_b': _L2_gnn_in['pred_b'], 'L3_gnn_W': _L3_gnn_in['W'], 'L3_gnn_b': _L3_gnn_in['b']}

def reference(x, src, dst, edge_attr_3, edge_attr_48, edge_attr_8, L0_gnn_W1, L0_gnn_b1, L0_gnn_W2, L0_gnn_b2, L1_gnn_fc0_w1, L1_gnn_fc0_b1, L1_gnn_fc0_w2, L1_gnn_fc0_b2, L1_gnn_fc1_w1, L1_gnn_fc1_b1, L1_gnn_fc1_w2, L1_gnn_fc1_b2, L1_gnn_bn0_gs, L1_gnn_bn0_bs, L1_gnn_bn0_gv, L1_gnn_bn1_gs, L1_gnn_bn1_bs, L2_gnn_edge_w, L2_gnn_edge_b, L2_gnn_root_w, L2_gnn_root_b, L2_gnn_bn_gamma, L2_gnn_bn_beta, L2_gnn_pred_w, L2_gnn_pred_b, L3_gnn_W, L3_gnn_b):
    import jax
    import jax.numpy as jnp

    def _L0_gnn_ref(x, edge_index, W1, b1, W2, b2):
        import jax, jax.numpy as jnp
        import numpy as np
        STALK_DIM = 16
        N_NODES = 6250
        N_EDGES = 50000
        HIDDEN = 64
        d = x.shape[1]
        n = x.shape[0]
        src, dst = (edge_index[0], edge_index[1])
        xs, xd = (x[src], x[dst])

        def reflection(a, b):
            h = jax.nn.relu(jnp.concatenate([a, b], axis=1) @ W1.T + b1)
            return h @ W2.T + b2

        def householder(v):
            vn = v / jnp.maximum(jnp.linalg.norm(v, axis=1, keepdims=True), 1e-12)
            return jnp.eye(d, dtype=v.dtype)[None] - 2.0 * vn[:, :, None] * vn[:, None, :]
        F_s = householder(reflection(xs, xd))
        F_d = householder(reflection(xd, xs))
        L_sd = -jnp.einsum('eki,ekj->eij', F_s, F_d)
        ones_e = jnp.ones(src.shape[0], dtype=x.dtype)
        deg = jnp.zeros(n, dtype=x.dtype).at[src].add(ones_e).at[dst].add(ones_e)
        deg_inv_sqrt = 1.0 / jnp.sqrt(jnp.maximum(deg, 1e-05))
        coef = deg_inv_sqrt[src] * deg_inv_sqrt[dst]
        msg_s = coef[:, None] * jnp.einsum('eij,ej->ei', L_sd, xd)
        msg_d = coef[:, None] * jnp.einsum('eji,ej->ei', L_sd, xs)
        out = x - jnp.zeros_like(x).at[src].add(msg_s) - jnp.zeros_like(x).at[dst].add(msg_d)
        return jax.nn.relu(out)

    def _L1_gnn_ref(node_attr, edge_attr, edge_vec, fc0_w1, fc0_b1, fc0_w2, fc0_b2, fc1_w1, fc1_b1, fc1_w2, fc1_b2, bn0_gs, bn0_bs, bn0_gv, bn1_gs, bn1_bs, edge_index):
        import jax, jax.numpy as jnp
        import numpy as np
        NS, NV = (16, 4)
        EPS = 1e-05
        N_NODES, N_EDGES = (5000, 50000)

        def _bn_scalar(x, g, b):
            m = x.mean(0)
            v = ((x - m) ** 2).mean(0)
            return (x - m) / jnp.sqrt(v + EPS) * g + b

        def _seg_mean(x, idx, n):
            s = jax.ops.segment_sum(x, idx, num_segments=n)
            c = jax.ops.segment_sum(jnp.ones((idx.shape[0],), x.dtype), idx, num_segments=n)
            return s / jnp.maximum(c, 1.0)[:, None]

        def _edge_weights(edge_attr, w1, b1, w2, b2):
            h = jax.nn.relu(edge_attr @ w1 + b1)
            return h @ w2 + b2

        def _forward(node_attr, edge_attr, edge_vec, fc0_w1, fc0_b1, fc0_w2, fc0_b2, fc1_w1, fc1_b1, fc1_w2, fc1_b2, bn0_gs, bn0_bs, bn0_gv, bn1_gs, bn1_bs, edge_index):
            N = node_attr.shape[0]
            E = edge_attr.shape[0]
            src, dst = (edge_index[0], edge_index[1])
            rhat = edge_vec / (jnp.linalg.norm(edge_vec, axis=-1, keepdims=True) + 1e-12)
            sh1 = rhat * float(np.sqrt(3.0))
            w = _edge_weights(edge_attr, fc0_w1, fc0_b1, fc0_w2, fc0_b2)
            wa = w[:, :NS * NS].reshape(E, NS, NS)
            wb = w[:, NS * NS:].reshape(E, NS, NV)
            x = node_attr[dst]
            inv = float(1.0 / np.sqrt(NS))
            msg_s = jnp.einsum('ei,eij->ej', x, wa) * inv
            msg_v = jnp.einsum('ei,eij,ec->ejc', x, wb, sh1) * inv
            msg = jnp.concatenate([msg_s, msg_v.reshape(E, NV * 3)], axis=-1)
            out = _seg_mean(msg, src, N)
            s0 = _bn_scalar(out[:, :NS], bn0_gs, bn0_bs)
            v0 = out[:, NS:].reshape(N, NV, 3)
            vn = jnp.sqrt((v0 ** 2).mean(axis=(0, 2)) + EPS)
            v0 = v0 / vn[None, :, None] * bn0_gv[None, :, None]
            w = _edge_weights(edge_attr, fc1_w1, fc1_b1, fc1_w2, fc1_b2)
            wa = w[:, :NS * NS].reshape(E, NS, NS)
            wb = w[:, NS * NS:].reshape(E, NV, NS)
            s = s0[dst]
            v = v0[dst]
            path_a = jnp.einsum('ei,eij->ej', s, wa)
            path_b = jnp.einsum('eic,ec,eij->ej', v, sh1, wb) * float(1.0 / np.sqrt(3.0))
            msg = (path_a + path_b) * float(1.0 / np.sqrt(NS + NV))
            node1 = _seg_mean(msg, src, N)
            return _bn_scalar(node1, bn1_gs, bn1_bs)
        return _forward(node_attr, edge_attr, edge_vec, fc0_w1, fc0_b1, fc0_w2, fc0_b2, fc1_w1, fc1_b1, fc1_w2, fc1_b2, bn0_gs, bn0_bs, bn0_gv, bn1_gs, bn1_bs, edge_index)

    def _L2_gnn_ref(x, edge_index, edge_attr, edge_w, edge_b, root_w, root_b, bn_gamma, bn_beta, pred_w, pred_b):
        import jax, jax.numpy as jnp
        import numpy as np
        N_NODES = 6250
        N_EDGES = 50000
        D = 16
        E_FEAT = 8
        N_LAYERS = 3
        BN_EPS = 1e-05

        def _nnconv(x, src, dst, edge_attr, ew, eb, rw, rb):
            W = (edge_attr @ ew + eb).reshape(edge_attr.shape[0], x.shape[1], rw.shape[1])
            xj = x[src]
            msg = jnp.einsum('ei,eio->eo', xj, W)
            agg = jax.ops.segment_sum(msg, dst, num_segments=x.shape[0])
            return agg + x @ rw + rb

        def _batchnorm(x, gamma, beta):
            mean = jnp.mean(x, axis=0)
            var = jnp.mean(jnp.square(x - mean), axis=0)
            return (x - mean) * jax.lax.rsqrt(var + BN_EPS) * gamma + beta
        src, dst = (edge_index[0], edge_index[1])
        h = x
        for i in range(N_LAYERS - 1):
            h = _nnconv(h, src, dst, edge_attr, edge_w[i], edge_b[i], root_w[i], root_b[i])
            h = _batchnorm(h, bn_gamma[i], bn_beta[i])
            h = jax.nn.relu(h)
        h = _nnconv(h, src, dst, edge_attr, edge_w[-1], edge_b[-1], root_w[-1], root_b[-1])
        h = jax.nn.relu(h)
        return h @ pred_w + pred_b

    def _L3_gnn_ref(x, edge_index, W, b):
        import jax, jax.numpy as jnp
        import numpy as np
        N_NODES = 125000
        n = x.shape[0]
        row, col = (edge_index[0], edge_index[1])
        h = x @ W
        deg = jax.ops.segment_sum(jnp.ones_like(col, dtype=h.dtype), col, num_segments=n) + 1.0
        dinv = jax.lax.rsqrt(deg)
        norm = dinv[row] * dinv[col]
        msgs = h[row] * norm[:, None]
        agg = jax.ops.segment_sum(msgs, col, num_segments=n)
        out = agg + h * (dinv * dinv)[:, None] + b
        return out
    edge_index = jnp.stack([src, dst])
    x = _layernorm(x + _L0_gnn_ref(x, edge_index, L0_gnn_W1, L0_gnn_b1, L0_gnn_W2, L0_gnn_b2), axis=-1)
    x = _layernorm(x + _L1_gnn_ref(x, edge_attr_48, edge_attr_3, L1_gnn_fc0_w1, L1_gnn_fc0_b1, L1_gnn_fc0_w2, L1_gnn_fc0_b2, L1_gnn_fc1_w1, L1_gnn_fc1_b1, L1_gnn_fc1_w2, L1_gnn_fc1_b2, L1_gnn_bn0_gs, L1_gnn_bn0_bs, L1_gnn_bn0_gv, L1_gnn_bn1_gs, L1_gnn_bn1_bs, edge_index), axis=-1)
    x = _layernorm(x + _L2_gnn_ref(x, edge_index, edge_attr_8, L2_gnn_edge_w, L2_gnn_edge_b, L2_gnn_root_w, L2_gnn_root_b, L2_gnn_bn_gamma, L2_gnn_bn_beta, L2_gnn_pred_w, L2_gnn_pred_b), axis=-1)
    x = _layernorm(x + _L3_gnn_ref(x, edge_index, L3_gnn_W, L3_gnn_b), axis=-1)
    return x

_drawn_inputs = setup_inputs


def setup_inputs(seed=0):
    import zlib

    import numpy as np

    out = dict(_drawn_inputs(seed))
    spreads = {'L0_gnn_b1': (0.0, 0.8),
     'L0_gnn_b2': (0.0, 0.616),
     'L1_gnn_fc0_b1': (0.0, 0.1),
     'L1_gnn_fc0_b2': (0.0, 0.1),
     'L1_gnn_fc1_b1': (0.0, 0.1),
     'L1_gnn_fc1_b2': (0.0, 0.1),
     'L1_gnn_bn0_gs': (1.0, 0.2),
     'L1_gnn_bn0_bs': (0.0, 0.1),
     'L1_gnn_bn0_gv': (1.0, 0.2),
     'L1_gnn_bn1_gs': (1.0, 0.2),
     'L1_gnn_bn1_bs': (0.0, 0.1),
     'L2_gnn_bn_gamma': (1.0, 0.2),
     'L2_gnn_bn_beta': (0.0, 0.1),
     'L3_gnn_b': (0.0, 0.1)}
    factors = {'L2_gnn_root_b': 5.174}
    for name, (base, spread) in spreads.items():
        noise = np.random.default_rng([zlib.crc32(name.encode()), seed]).standard_normal(out[name].shape)
        drawn = base * np.exp(spread * noise) if base else spread * noise
        out[name] = jnp.asarray(drawn.astype(out[name].dtype))
    for name, factor in factors.items():
        out[name] = (out[name] * factor).astype(out[name].dtype)
    return out
```

```python
from contextlib import ExitStack, contextmanager

import concourse.bass as bass
from concourse import mybir

F32 = mybir.dt.float32
BF16 = mybir.dt.bfloat16
I32 = mybir.dt.int32
ALU = mybir.AluOpType
ACT = mybir.ActivationFunctionType
AX = mybir.AxisListType

P = 128
N = 12500
E = 400000
D = 16
NB = -(-N // P)
LAST = N - (NB - 1) * P
G = 8
RING = 4
C = -(-(E // P + NB) // (G * RING)) * RING
T = C * G
RD = 11
RS = 54
EP = E // P
SG = 25
SC = EP // SG
EPS = 1e-5
TB = 32


def run_chunks(eng, total, ring, body):
    head = ring + total % ring
    for c in range(head):
        body(c, c % ring, c // ring)
    with eng.Fori(0, (total - head) // ring) as i:
        for h in range(head, head + ring):
            body(i * ring + h, h % ring, i + h // ring)


def wait_past(eng, sem, value):
    if not isinstance(value, int) or value > 0:
        eng.wait_ge(sem, value)


class Chain:

    def __init__(self, eng, sem, per=0):
        self.eng, self.sem, self.per, self.base, self.n = eng, sem, per, 0, 0

    def turn(self, c):
        self.base, self.n = (c * self.per if self.per else 0), 0

    def link(self, ins):
        ins.then_inc(self.sem, 1)
        self.n += 1
        self.eng.wait_ge(self.sem, self.base + self.n)

    def end(self):
        assert not self.per or self.n == self.per, (self.n, self.per)


@contextmanager
def phase_semaphores(nc, tag):
    with ExitStack() as ctx:
        held = []

        def sem(name):
            held.append(ctx.enter_context(nc.semaphore(f"{tag}_{name}")))
            return held[-1]
        yield sem
        with nc.Block() as block:
            @block.sync
            def _(sp):
                for s in held:
                    sp.sem_clear(s)


def make_consts(nc, ctx):
    k = {}
    for name, shape, dt in (("ident", [P, P], F32), ("identb", [P, P], BF16), ("ones", [P, P], F32),
                            ("before", [P, P], F32), ("iota", [P, P], F32), ("tile_no", [P, TB], F32),
                            ("in_last", [P, 1], F32), ("part", [P, 1], F32)):
        k[name] = ctx.enter_context(nc.sbuf_tensor(name, shape, dt))
    s_fill = ctx.enter_context(nc.semaphore("s_const_fill"))
    with nc.Block() as block:
        @block.gpsimd
        def _(pool):
            nc.gpsimd.memset(k["ident"][:, :], 0.0).then_inc(s_fill, 1)
            nc.gpsimd.memset(k["identb"][:, :], 0.0).then_inc(s_fill, 1)
            nc.gpsimd.memset(k["ones"][:, :], 1.0).then_inc(s_fill, 1)
            nc.gpsimd.memset(k["before"][:, :], 1.0).then_inc(s_fill, 1)
            nc.gpsimd.iota(k["iota"][:, :], [[1, P]], base=0, channel_multiplier=0,
                           allow_small_or_imprecise_dtypes=True).then_inc(s_fill, 1)
            nc.gpsimd.iota(k["tile_no"][:, :], [[1, TB]], base=0, channel_multiplier=TB,
                           allow_small_or_imprecise_dtypes=True).then_inc(s_fill, 1)
            nc.gpsimd.iota(k["part"][:, :], [[1, 1]], base=0, channel_multiplier=1,
                           allow_small_or_imprecise_dtypes=True).then_inc(s_fill, 1)
            pool.wait_ge(s_fill, 7)
            nc.gpsimd.tensor_scalar(k["in_last"][:, :], k["part"][:, :], float(LAST), None, ALU.is_lt)\
                .then_inc(s_fill, 1)
            for name in ("ident", "identb"):
                nc.gpsimd.affine_select(out=k[name][:, :], in_=k[name][:, :], compare_op=ALU.not_equal,
                                        fill=1.0, base=0, pattern=[[-1, P]], channel_multiplier=1)\
                    .then_inc(s_fill, 1)
            nc.gpsimd.affine_select(out=k["before"][:, :], in_=k["before"][:, :], compare_op=ALU.is_gt,
                                    fill=0.0, base=0, pattern=[[1, P]], channel_multiplier=-1)\
                .then_inc(s_fill, 1)
            pool.wait_ge(s_fill, 11)
    return k


def sort_edges(nc, k, src, dst, ea3, ea48, ea8, rec_d, rec_s, blk_dram, blk, deg, rows_out):
    keys = ("s", "d")
    src_v = src.rearrange("(p t) -> p t", p=P)
    dst_v = dst.rearrange("(p t) -> p t", p=P)
    ea3_v = ea3.rearrange("(p t) f -> p t f", p=P)
    ea8_v = ea8.rearrange("(p t) f -> p t f", p=P)
    ea48_v = ea48.rearrange("(p t) f -> p t f", p=P)
    with ExitStack() as ctx:
        sem = ctx.enter_context(phase_semaphores(nc, "sort"))

        def sb(name, shape, dt=F32):
            return ctx.enter_context(nc.sbuf_tensor(name, shape, dt))

        node = {"s": sb("node_s", [P, EP], I32), "d": sb("node_d", [P, EP], I32)}
        lo = {q: sb(f"lo_{q}", [P, EP]) for q in keys}
        hi = {q: sb(f"hi_{q}", [P, EP]) for q in keys}
        place = {q: sb(f"place_{q}", [P, NB]) for q in keys}

        with ExitStack() as ph:
            oh_lo = {q: ph.enter_context(nc.sbuf_tensor(f"oh_lo_{q}", [P, 2, 5, P], BF16)) for q in keys}
            oh_hi = {q: ph.enter_context(nc.sbuf_tensor(f"oh_hi_{q}", [P, 2, 5, NB], BF16)) for q in keys}
            hist = {q: ph.enter_context(nc.psum_tensor(f"hist_{q}", [P, 512], F32)) for q in keys}
            count = {q: ph.enter_context(nc.psum_tensor(f"count_{q}", [P, 512], F32)) for q in keys}
            part = ph.enter_context(nc.psum_tensor("part_base", [P, 2, 256], F32))
            scan = {n: ph.enter_context(nc.sbuf_tensor(f"scan_{n}", [P, NB], F32))
                    for n in ("h", "tiles", "end", "one")}
            tot = ph.enter_context(nc.sbuf_tensor("scan_tot", [P, NB], I32))
            tile_ge = ph.enter_context(nc.sbuf_tensor("tile_ge", [P, TB, NB], F32))
            tile_blk = ph.enter_context(nc.sbuf_tensor("tile_blk", [P, TB], F32))
            tile_blk_i = ph.enter_context(nc.sbuf_tensor("tile_blk_i", [P, 2, TB], I32))
            blank_d = ph.enter_context(nc.sbuf_tensor("blank_d", [P, G, RD], F32))
            blank_s = ph.enter_context(nc.sbuf_tensor("blank_s", [P, G, RS], F32))
            idx_in, blanks_set, blanks_out = sem("idx_in"), sem("blanks_set"), sem("blanks_out")
            oh_ready, oh_used, hist_chain = sem("oh_ready"), sem("oh_used"), sem("hist_chain")
            h_ready, part_ready, blk_ready, blk_out, blk_in = (
                sem("h_ready"), sem("part_ready"), sem("blk_ready"), sem("blk_out"), sem("blk_in"))
            HT = 5
            HC = EP // HT

            with nc.Block() as block:
                @block.sync
                def _(sp):
                    sp.dma_start(node["s"][:, :], src_v).then_inc(idx_in, 16)
                    sp.dma_start(node["d"][:, :], dst_v).then_inc(idx_in, 16)
                    sp.wait_ge(blanks_set, 4)
                    sp.dma_start(rec_d.rearrange("(c p g) f -> p c (g f)", p=P, g=G),
                                 blank_d[:, :, :].rearrange("p g f -> p (g f)").unsqueeze(1)
                                 .to_broadcast([P, C, G * RD])).then_inc(blanks_out, 16)
                    sp.dma_start(rec_s.rearrange("(c p g) f -> p c (g f)", p=P, g=G),
                                 blank_s[:, :, :].rearrange("p g f -> p (g f)").unsqueeze(1)
                                 .to_broadcast([P, C, G * RS])).then_inc(blanks_out, 16)
                    for n, q in enumerate(keys):
                        sp.wait_ge(blk_ready, n + 1)
                        sp.dma_start(blk_dram[q].rearrange("(p t) -> p t", t=TB),
                                     tile_blk_i[0:T // TB, n, :]).then_inc(blk_out, 16)
                        sp.wait_ge(blk_out, 16 * (n + 1))
                        sp.dma_start(blk[q][0:1, :], blk_dram[q].rearrange("(a t) -> a t", a=1))\
                            .then_inc(blk_in, 16)
                    sp.wait_ge(blk_in, 32)
                    sp.wait_ge(blanks_out, 32)

                @block.gpsimd
                def _(pool):
                    nc.gpsimd.memset(blank_d[:, :, :], 0.0).then_inc(blanks_set, 1)
                    nc.gpsimd.memset(blank_s[:, :, :], 0.0).then_inc(blanks_set, 1)
                    pool.wait_ge(blanks_set, 2)
                    nc.gpsimd.memset(blank_d[:, :, 1:2], -1.0).then_inc(blanks_set, 1)
                    nc.gpsimd.memset(blank_s[:, :, 1:2], -1.0).then_inc(blanks_set, 1)

                @block.tensor
                def _(pe):
                    def body(c, slot, turn, first=False, last=False):
                        pe.wait_ge(oh_ready, c + 1)
                        for q in keys:
                            nc.tensor.matmul(hist[q][:, 0:HT * NB], k["identb"][:, :],
                                             oh_hi[q][:, slot, :, :].rearrange("p t b -> p (t b)"),
                                             start=first, stop=last)
                            for t in range(HT):
                                ins = nc.tensor.matmul(count[q][:, 0:NB], oh_lo[q][:, slot, t, :],
                                                       oh_hi[q][:, slot, t, :],
                                                       start=first and t == 0, stop=last and t == HT - 1)
                        ins.then_inc(oh_used, 1)

                    body(0, 0, 0, first=True)
                    with pe.Fori(0, (HC - 3) // 2) as i:
                        body(i * 2 + 1, 1, 0)
                        body(i * 2 + 2, 0, 0)
                    body(HC - 2, (HC - 2) % 2, 0)
                    body(HC - 1, (HC - 1) % 2, 0, last=True)
                    for n, q in enumerate(keys):
                        pe.wait_ge(h_ready, n + 1)
                        nc.tensor.matmul(part[:, 0, 0:NB], k["before"][:, :], scan["h"][:, :],
                                         start=True, stop=True)
                        nc.tensor.matmul(part[:, 1, 0:NB], k["ones"][:, :], scan["h"][:, :],
                                         start=True, stop=True).then_inc(part_ready, 1)

                @block.vector
                def _(dve):
                    chain = Chain(dve, hist_chain)
                    link = chain.link
                    dve.wait_ge(idx_in, 32)
                    for q in keys:
                        link(nc.vector.tensor_scalar(hi[q][:, :].bitcast(I32), node[q][:, :], 7, None,
                                                     ALU.arith_shift_right))
                        link(nc.vector.tensor_scalar(lo[q][:, :].bitcast(I32), node[q][:, :], P - 1, None,
                                                     ALU.bitwise_and))
                        link(nc.vector.tensor_copy(hi[q][:, :], hi[q][:, :].bitcast(I32)))
                        link(nc.vector.tensor_copy(lo[q][:, :], lo[q][:, :].bitcast(I32)))

                    def body(c, slot, turn):
                        wait_past(dve, oh_used, c - 1)
                        for q in keys:
                            nc.vector.tensor_tensor(
                                oh_lo[q][:, slot, :, :],
                                lo[q][:, bass.ds(c * HT, HT)].unsqueeze(2).to_broadcast([P, HT, P]),
                                k["iota"][:, :].unsqueeze(1).to_broadcast([P, HT, P]), ALU.is_equal)
                            ins = nc.vector.tensor_tensor(
                                oh_hi[q][:, slot, :, :],
                                hi[q][:, bass.ds(c * HT, HT)].unsqueeze(2).to_broadcast([P, HT, NB]),
                                k["iota"][:, 0:NB].unsqueeze(1).to_broadcast([P, HT, NB]), ALU.is_equal)
                        ins.then_inc(oh_ready, 1)

                    run_chunks(dve, HC, 2, body)
                    dve.wait_ge(oh_used, HC)
                    link(nc.vector.memset(scan["one"][:, :], 1.0))
                    for n, q in enumerate(keys):
                        link(nc.vector.tensor_copy(deg[q][:, :], count[q][:, 0:NB]))
                        if n:
                            dve.wait_ge(part_ready, n)
                        nc.vector.tensor_reduce(scan["h"][:, :],
                                                hist[q][:, 0:HT * NB].rearrange("p (t b) -> p b t", t=HT),
                                                AX.X, ALU.add).then_inc(h_ready, 1)
                        dve.wait_ge(part_ready, n + 1)
                        link(nc.vector.tensor_scalar(tot[:, :], part[:, 1, 0:NB], float(P - 1), None,
                                                     ALU.add))
                        link(nc.vector.tensor_scalar(tot[:, :], tot[:, :], 7, None, ALU.arith_shift_right))
                        link(nc.vector.tensor_copy(scan["tiles"][:, :], tot[:, :]))
                        link(nc.vector.tensor_tensor_scan(scan["end"][:, :], scan["one"][:, :],
                                                          scan["tiles"][:, :], 0.0, ALU.mult, ALU.add))
                        link(nc.vector.tensor_sub(scan["tiles"][:, :], scan["end"][:, :],
                                                  scan["tiles"][:, :]))
                        link(nc.vector.scalar_tensor_tensor(place[q][:, :], scan["tiles"][:, :], float(P),
                                                            part[:, 0, 0:NB], ALU.mult, ALU.add))
                        link(nc.vector.tensor_tensor(
                            tile_ge[:, :, :], k["tile_no"][:, :].unsqueeze(2).to_broadcast([P, TB, NB]),
                            scan["end"][:, :].unsqueeze(1).to_broadcast([P, TB, NB]), ALU.is_ge))
                        link(nc.vector.tensor_reduce(tile_blk[:, :], tile_ge[:, :, :], AX.X, ALU.add))
                        nc.vector.tensor_scalar(tile_blk_i[:, n, :], tile_blk[:, :], float(NB - 1), None,
                                                ALU.min).then_inc(blk_ready, 1)
                    dve.wait_ge(blk_ready, 2)

        oh = {q: sb(f"rank_oh_{q}", [P, SG, NB], BF16) for q in keys}
        junk = {q: sb(f"rank_junk_{q}", [P, NB]) for q in keys}
        pos = {q: sb(f"pos_{q}", [P, SG]) for q in keys}
        pos_i = {q: sb(f"pos_i_{q}", [P, SG], I32) for q in keys}
        low = {q: sb(f"low_{q}", [P, SG], I32) for q in keys}
        tno = {q: sb(f"tno_{q}", [P, SG], I32) for q in keys}
        row = {q: sb(f"row_{q}", [P, 2, SG], I32) for q in keys}
        out_s, out_d = sb("out_s", [P, 2, SG, RS]), sb("out_d", [P, 2, SG, RD])
        vec = sb("edge_vec", [P, 2, SG, 3])
        sq, nrm, rcp = sb("vec_sq", [P, SG, 3]), sb("vec_norm", [P, SG]), sb("vec_rcp", [P, SG])
        attr_in = [sem(f"attr_in{h}") for h in range(2)]
        rows_ready, rank_chain, sq_ready, norm_ready, pool_turn = (
            sem("rows_ready"), sem("rank_chain"), sem("sq_ready"), sem("norm_ready"), sem("pool_turn"))

        with nc.Block() as block:
            @block.sync
            def _(sp):
                def body(c, slot, turn):
                    wait_past(sp, rows_out[slot], turn * (2 * SG * 16))
                    sp.dma_start(out_s[:, slot, :, 6:RS], ea48_v[:, bass.ds(c * SG, SG), :])\
                        .then_inc(attr_in[slot], 16)
                    sp.dma_start(out_d[:, slot, :, 2:10], ea8_v[:, bass.ds(c * SG, SG), :])\
                        .then_inc(attr_in[slot], 16)
                    sp.dma_start(vec[:, slot, :, :], ea3_v[:, bass.ds(c * SG, SG), :])\
                        .then_inc(attr_in[slot], 16)
                run_chunks(sp, SC, 2, body)

            @block.scalar
            def _(act):
                def body(c, slot, turn):
                    act.wait_ge(sq_ready, c + 1)
                    nc.scalar.activation(nrm[:, :], nrm[:, :], ACT.Sqrt).then_inc(norm_ready, 1)
                run_chunks(act, SC, 2, body)

            @block.vector
            def _(dve):
                chain = Chain(dve, rank_chain, per=2 * SG * 2 + 28)
                link = chain.link

                def body(c, slot, turn):
                    chain.turn(c)
                    dve.wait_ge(attr_in[slot], (turn + 1) * 48)
                    link(nc.vector.tensor_mul(sq[:, :, :], vec[:, slot, :, :], vec[:, slot, :, :]))
                    nc.vector.tensor_reduce(nrm[:, :], sq[:, :, :], AX.X, ALU.add).then_inc(sq_ready, 1)
                    for q in keys:
                        link(nc.vector.tensor_tensor(
                            oh[q][:, :, :],
                            hi[q][:, bass.ds(c * SG, SG)].unsqueeze(2).to_broadcast([P, SG, NB]),
                            k["iota"][:, 0:NB].unsqueeze(1).to_broadcast([P, SG, NB]), ALU.is_equal))
                    for t in range(SG):
                        for q in keys:
                            link(nc.vector.tensor_tensor_reduce(
                                junk[q][:, :], oh[q][:, t, :], place[q][:, :], 1.0, 0.0, ALU.mult,
                                ALU.add, pos[q][:, t:t + 1]))
                            link(nc.vector.tensor_add(place[q][:, :], place[q][:, :], oh[q][:, t, :]))
                    for q in keys:
                        link(nc.vector.tensor_copy(pos_i[q][:, :], pos[q][:, :]))
                        link(nc.vector.tensor_scalar(low[q][:, :], pos_i[q][:, :], P - 1, 3,
                                                     ALU.bitwise_and, ALU.logical_shift_left))
                        link(nc.vector.tensor_scalar(tno[q][:, :], pos_i[q][:, :], 7, G - 1,
                                                     ALU.arith_shift_right, ALU.bitwise_and))
                        link(nc.vector.tensor_scalar(pos_i[q][:, :], pos_i[q][:, :], 10, 10,
                                                     ALU.arith_shift_right, ALU.logical_shift_left))
                        link(nc.vector.tensor_tensor(low[q][:, :], low[q][:, :], tno[q][:, :],
                                                     ALU.bitwise_or))
                        link(nc.vector.tensor_tensor(row[q][:, slot, :], low[q][:, :], pos_i[q][:, :],
                                                     ALU.bitwise_or))
                    link(nc.vector.tensor_copy(out_s[:, slot, :, 0:1].bitcast(I32),
                                               node["d"][:, bass.ds(c * SG, SG)].unsqueeze(2)))
                    link(nc.vector.tensor_copy(out_d[:, slot, :, 0:1].bitcast(I32),
                                               node["s"][:, bass.ds(c * SG, SG)].unsqueeze(2)))
                    link(nc.vector.tensor_copy(out_s[:, slot, :, 1:2],
                                               lo["s"][:, bass.ds(c * SG, SG)].unsqueeze(2)))
                    link(nc.vector.tensor_copy(out_d[:, slot, :, 1:2],
                                               lo["d"][:, bass.ds(c * SG, SG)].unsqueeze(2)))
                    link(nc.vector.tensor_copy(out_s[:, slot, :, 2:3].bitcast(I32),
                                               row["d"][:, slot, :].unsqueeze(2)))
                    link(nc.vector.memset(out_d[:, slot, :, 10:11], 1.0))
                    dve.wait_ge(norm_ready, c + 1)
                    link(nc.vector.tensor_scalar(nrm[:, :], nrm[:, :], 1e-12, None, ALU.add))
                    link(nc.vector.reciprocal(rcp[:, :], nrm[:, :]))
                    link(nc.vector.tensor_mul(vec[:, slot, :, :], vec[:, slot, :, :],
                                              rcp[:, :].unsqueeze(2).to_broadcast([P, SG, 3])))
                    link(nc.vector.tensor_scalar(out_s[:, slot, :, 3:6], vec[:, slot, :, :], 3.0 ** 0.5,
                                                 None, ALU.mult))
                    link(nc.vector.memset(sq[:, 0:1, 0:1], 0.0))
                    link(nc.vector.memset(sq[:, 0:1, 0:1], 0.0))
                    link(nc.vector.memset(sq[:, 0:1, 0:1], 0.0))
                    dve.sem_inc(rows_ready, 1)
                    chain.end()
                run_chunks(dve, SC, 2, body)

            @block.gpsimd
            def _(pool):
                def body(c, slot, turn):
                    pool.wait_ge(rows_ready, c + 1)
                    pool.sem_inc(pool_turn, 1)
                    for t in range(SG):
                        nc.gpsimd.indirect_dma_start(
                            rec_s, bass.IndirectOffsetOnAxis(ap=row["s"][:, slot, t:t + 1], axis=0),
                            out_s[:, slot, t, :], None).then_inc(rows_out[slot], 16)
                        nc.gpsimd.indirect_dma_start(
                            rec_d, bass.IndirectOffsetOnAxis(ap=row["d"][:, slot, t:t + 1], axis=0),
                            out_d[:, slot, t, :], None).then_inc(rows_out[slot], 16)
                run_chunks(pool, SC, 2, body)
                pool.wait_ge(rows_out[0], (SC + 1) // 2 * (2 * SG * 16))
                pool.wait_ge(rows_out[1], SC // 2 * (2 * SG * 16))


def edge_pass(nc, k, tag, kind, rec, rw, table, tw, blk, acc, f, w, rows_in):
    tensor = kind in ("tensor0", "tensor1")
    sheaf = kind == "sheaf"
    ni, no = {"tensor0": (D, 20), "tensor1": (20, D)}.get(kind, (0, 0))
    bank = 512
    with ExitStack() as ctx:
        sem = ctx.enter_context(phase_semaphores(nc, tag))

        def sb(name, shape, dt=F32):
            return ctx.enter_context(nc.sbuf_tensor(f"{tag}_{name}", shape, dt))

        def ps(name, shape, dt=F32):
            return ctx.enter_context(nc.psum_tensor(f"{tag}_{name}", shape, dt))

        recs = sb("recs", [P, RING, G, rw])
        rows = sb("rows", [P, RING, G, tw])
        onehot = sb("onehot", [P, RING, G, P])
        if f == 144:
            sums = ps("sums", [P, 2, 3 * bank])
        else:
            sums = ps("sums", [P, 2, bank])

        def sum_of(par, g):
            at = (g // 3) * bank + (g % 3) * f if f == 144 else g * f
            return sums[:, par, at:at + f]

        recs_in = [sem(f"recs_in{r}") for r in range(RING)]
        pool_turn, acc_zero, onehots_made, values_made, sums_made, added = (
            sem("pool_turn"), sem("acc_zero"), sem("onehots_made"), sem("values_made"),
            sem("sums_made"), sem("added"))
        if kind == "outer":
            values = sb("values", [P, 2, G, f])
        if tensor:
            attr_t = sb("attr_t", [48, 2, bank])
            hidden_t = sb("hidden_t", [64, 2, bank])
            prod = sb("prod", [P, 2, 2, no, ni])
            mixed = sb("mixed", [P, G, no])
            values = sb("values", [P, 2, G, f])
            xin = sb("xin", [P, G, 20])
            vsh = sb("vsh", [P, G, 4, 3])
            front = ps("front", [P, 2, bank])
            weights = ps("weights", [P, 4, bank])
            pe_turn = sem("pe_turn")
            attr_tp, attr_copied, hidden_made, hidden_copied, weights_made, weights_used, tensor_chain = (
                sem("attr_tp"), sem("attr_copied"), sem("hidden_made"), sem("hidden_copied"),
                sem("weights_made"), sem("weights_used"), sem("tensor_chain"))
        if sheaf:
            onehot_t = sb("onehot_t", [P, 2, bank])
            hid = sb("hid", [P, 2, bank])
            hid_t = sb("hid_t", [P, 2, bank])
            turned = ps("turned", [P, 2, bank])
            hid_ps = ps("hid_ps", [P, 2, bank])
            out_ps = ps("out_ps", [P, 2, bank])
            aba = sb("aba", [P, G, 3, D])
            rcp = sb("rcp", [P, G, 3])
            dot = sb("dot", [P, G, 2])
            tmp = sb("tmp", [P, G, 2, D])
            values = sb("values", [P, 2, G, 2, D])
            oh_turned, oh_copied, hid_made, hid_relu, hid_turned, hid_copied, refl_made, sheaf_chain = (
                sem("oh_turned"), sem("oh_copied"), sem("hid_made"), sem("hid_relu"),
                sem("hid_turned"), sem("hid_copied"), sem("refl_made"), sem("sheaf_chain"))
            msg_out = [sem(f"msg_out{h}") for h in range(2)]

        with nc.Block() as block:
            @block.sync
            def _(sp):
                def body(c, slot, turn):
                    wait_past(sp, added, (c - RING + 1) * G)
                    sp.dma_start(recs[:, slot, :, :],
                                 rec[bass.ds(c * (P * G), P * G), :].rearrange("(p g) f -> p g f", g=G))\
                        .then_inc(recs_in[slot], 16)
                run_chunks(sp, C, RING, body)

            @block.gpsimd
            def _(pool):
                col = 2 if kind == "row" else 0

                def body(c, slot, turn):
                    pool.wait_ge(recs_in[slot], (turn + 1) * 16)
                    pool.sem_inc(pool_turn, 1)
                    for g in range(G):
                        nc.gpsimd.indirect_dma_start(
                            rows[:, slot, g, :], None, table,
                            bass.IndirectOffsetOnAxis(ap=recs[:, slot, g, col:col + 1].bitcast(I32), axis=0))\
                            .then_inc(rows_in[slot], 16)
                run_chunks(pool, C, RING, body)

            @block.scalar
            def _(act):
                def tensor_body(c, slot, turn):
                    for h in range(2):
                        act.wait_ge(attr_tp, c * 2 + h + 1)
                        wait_past(act, hidden_made, c * 2 + h - 1)
                        nc.scalar.copy(attr_t[:, h, :], front[0:48, h, :]).then_inc(attr_copied, 1)
                    for h in range(2):
                        act.wait_ge(hidden_made, c * 2 + h + 1)
                        wait_past(act, weights_made, c * 4 + 2 * h - 2)
                        nc.scalar.activation(hidden_t[0:48, h, :], front[0:48, h, :], ACT.Relu,
                                             bias=w["b1"][:, 0:1]).then_inc(hidden_copied, 1)

                def sheaf_body(c, slot, turn):
                    for h in range(2):
                        act.wait_ge(oh_turned, c * 2 + h + 1)
                        wait_past(act, hid_made, c * 2 + h - 1)
                        nc.scalar.copy(onehot_t[:, h, :], turned[:, h, :]).then_inc(oh_copied, 1)
                    for h in range(2):
                        act.wait_ge(hid_made, c * 2 + h + 1)
                        wait_past(act, hid_turned, c * 2 + h - 1)
                        nc.scalar.activation(hid[:, h, :], hid_ps[:, h, :], ACT.Relu).then_inc(hid_relu, 1)
                    for h in range(2):
                        act.wait_ge(hid_turned, c * 2 + h + 1)
                        wait_past(act, refl_made, c)
                        nc.scalar.copy(hid_t[:, h, :], turned[:, h, :]).then_inc(hid_copied, 1)
                    if not isinstance(c, int) or c > 0:
                        store(c - 1, (slot - 1) % 2)

                def store(c, par):
                    act.wait_ge(values_made, c + 1)
                    act.dma_start(w["msg"][bass.ds(c * (P * G), P * G), :]
                                  .rearrange("(p g) f -> p g f", g=G), values[:, par, :, 1, :])\
                        .then_inc(msg_out[par], 16)

                if tensor:
                    act.wait_ge(acc_zero, 2)
                    run_chunks(act, C, RING, tensor_body)
                if sheaf:
                    run_chunks(act, C, RING, sheaf_body)
                    store(C - 1, (C - 1) % 2)
                    for par in range(2):
                        act.wait_ge(msg_out[par], 16 * (C // 2))

            @block.tensor
            def _(pe):
                def sum_up(c, slot):
                    par = slot % 2
                    if kind in ("plain", "row"):
                        pe.wait_ge(onehots_made, c + 1)
                    else:
                        pe.wait_ge(values_made, c + 1)
                    wait_past(pe, added, (c - 1) * G)
                    for g in range(G):
                        vals = (rows[:, slot, g, :] if kind in ("plain", "row") else
                                values[:, par, g, 0, :] if sheaf else values[:, par, g, :])
                        ins = nc.tensor.matmul(sum_of(par, g), onehot[:, slot, g, :], vals,
                                               start=True, stop=True)
                    ins.then_inc(sums_made, 1)

                def simple_body(c, slot, turn):
                    pe.wait_ge(rows_in[slot], (turn + 1) * (16 * G))
                    sum_up(c, slot)

                def tensor_body(c, slot, turn):
                    pe.wait_ge(recs_in[slot], (turn + 1) * 16)
                    for h in range(2):
                        wait_past(pe, hidden_copied, c * 2 + h - 1)
                        pe.sem_inc(pe_turn, 1)
                        for g in range(4):
                            ins = nc.tensor.transpose(front[0:48, h, g * P:(g + 1) * P],
                                                      recs[:, slot, 4 * h + g, 6:RS], k["ident"][:, :])
                        ins.then_inc(attr_tp, 1)
                    for h in range(2):
                        pe.wait_ge(attr_copied, c * 2 + h + 1)
                        pe.sem_inc(pe_turn, 1)
                        nc.tensor.matmul(front[0:48, h, :], w["w1"][:, :], attr_t[:, h, :],
                                         start=True, stop=True).then_inc(hidden_made, 1)
                    if not isinstance(c, int) or c > 0:
                        sum_up(c - 1, (slot - 1) % RING)
                    for j in range(4):
                        if j % 2 == 0:
                            pe.wait_ge(hidden_copied, c * 2 + j // 2 + 1)
                        wait_past(pe, weights_used, c * 4 + j - 1)
                        for t in range(2):
                            g = 2 * j + t
                            ins = nc.tensor.matmul(
                                weights[:, 2 * (j % 2) + t, 0:320],
                                hidden_t[0:49, g // 4, (g % 4) * P:(g % 4 + 1) * P], w["w2"][:, :],
                                start=True, stop=True)
                        ins.then_inc(weights_made, 1)

                def sheaf_body(c, slot, turn):
                    par = slot % 2
                    pe.wait_ge(onehots_made, c + 1)
                    for h in range(2):
                        wait_past(pe, hid_copied, c * 2 + h - 1)
                        for g in range(4):
                            ins = nc.tensor.transpose(turned[:, h, g * P:(g + 1) * P],
                                                      onehot[:, slot, 4 * h + g, :], k["ident"][:, :])
                        ins.then_inc(oh_turned, 1)
                    if not isinstance(c, int) or c > 1:
                        sum_up(c - 2, (slot - 2) % RING)
                    pe.wait_ge(rows_in[slot], (turn + 1) * (16 * G))
                    wait_past(pe, values_made, c - 1)
                    for g in range(G):
                        h = g // 4
                        b = pe.value_load(blk[0:1, bass.ds(c * G + g, 1)], min_val=0, max_val=NB - 1)
                        if g % 4 == 0:
                            pe.wait_ge(oh_copied, c * 2 + h + 1)
                            wait_past(pe, hid_relu, c * 2 + h - 1)
                        own = onehot_t[:, h, (g % 4) * P:(g % 4 + 1) * P]
                        nc.tensor.matmul(out_ps[:, par, g * D:(g + 1) * D], own,
                                         w["y"][:, bass.ds(b * D, D)], start=True, stop=True)
                        hp = hid_ps[:, h, (g % 4) * P:(g % 4 + 1) * P]
                        nc.tensor.matmul(hp, own, w["own"][:, bass.ds(b * P, P)], start=True, stop=False)
                        ins = nc.tensor.matmul(hp, k["ident"][:, :], rows[:, slot, g, D:D + P],
                                               start=False, stop=True)
                        if g % 4 == 3:
                            ins.then_inc(hid_made, 1)
                    for h in range(2):
                        pe.wait_ge(hid_relu, c * 2 + h + 1)
                        for g in range(4):
                            ins = nc.tensor.transpose(turned[:, h, g * P:(g + 1) * P],
                                                      hid[:, h, g * P:(g + 1) * P], k["ident"][:, :])
                        ins.then_inc(hid_turned, 1)
                    for g in range(G):
                        if g % 4 == 0:
                            pe.wait_ge(hid_copied, c * 2 + g // 4 + 1)
                        ins = nc.tensor.matmul(out_ps[:, par, G * D + g * 2 * D:G * D + (g + 1) * 2 * D],
                                               hid_t[:, g // 4, (g % 4) * P:(g % 4 + 1) * P],
                                               w["w2"][:, :], start=True, stop=True)
                    ins.then_inc(refl_made, 1)

                if tensor:
                    run_chunks(pe, C, RING, tensor_body)
                    sum_up(C - 1, (C - 1) % RING)
                elif sheaf:
                    run_chunks(pe, C, RING, sheaf_body)
                    sum_up(C - 2, (C - 2) % RING)
                    sum_up(C - 1, (C - 1) % RING)
                else:
                    run_chunks(pe, C, RING, simple_body)

            @block.vector
            def _(dve):
                nc.vector.memset(acc[:, :], 0.0).then_inc(acc_zero, 1)
                if tensor:
                    nc.vector.memset(hidden_t[:, :, :], 1.0).then_inc(acc_zero, 1)
                    dve.wait_ge(acc_zero, 2)
                else:
                    dve.wait_ge(acc_zero, 1)
                adds = Chain(dve, added, per=G)

                def add_up(c, slot):
                    adds.turn(c)
                    dve.wait_ge(sums_made, c + 1)
                    for g in range(G):
                        b = dve.value_load(blk[0:1, bass.ds(c * G + g, 1)], min_val=0, max_val=NB - 1)
                        at = acc[:, bass.ds(b * f, f)]
                        adds.link(nc.vector.tensor_add(at, at, sum_of(slot % 2, g)))
                    adds.end()

                def one_hots(c, slot, turn):
                    dve.wait_ge(recs_in[slot], (turn + 1) * 16)
                    nc.vector.tensor_tensor(onehot[:, slot, :, :],
                                            recs[:, slot, :, 1:2].to_broadcast([P, G, P]),
                                            k["iota"][:, :].unsqueeze(1).to_broadcast([P, G, P]),
                                            ALU.is_equal).then_inc(onehots_made, 1)

                def simple_body(c, slot, turn):
                    one_hots(c, slot, turn)
                    if kind == "outer":
                        dve.wait_ge(rows_in[slot], (turn + 1) * (16 * G))
                        nc.vector.tensor_mul(
                            values[:, slot % 2, :, :].rearrange("p g (a i) -> p g a i", i=D),
                            rows[:, slot, :, :].unsqueeze(2).to_broadcast([P, G, 9, D]),
                            recs[:, slot, :, 2:RD].unsqueeze(3).to_broadcast([P, G, 9, D]))\
                            .then_inc(values_made, 1)
                    if not isinstance(c, int) or c > 0:
                        add_up(c - 1, (slot - 1) % RING)

                chain = Chain(dve, tensor_chain, per={"tensor0": 2, "tensor1": 4}[kind]) if tensor else None

                def tensor_body(c, slot, turn):
                    one_hots(c, slot, turn)
                    dve.wait_ge(rows_in[slot], (turn + 1) * (16 * G))
                    chain.turn(c)
                    x = rows[:, slot, :, :]
                    sh = recs[:, slot, :, 3:6]
                    if kind == "tensor1":
                        chain.link(nc.vector.tensor_copy(xin[:, :, 0:D], rows[:, slot, :, 0:D]))
                        chain.link(nc.vector.tensor_mul(
                            vsh[:, :, :, :], rows[:, slot, :, D:28].rearrange("p g (i c) -> p g i c", c=3),
                            sh.unsqueeze(2).to_broadcast([P, G, 4, 3])))
                        chain.link(nc.vector.tensor_reduce(xin[:, :, D:20], vsh[:, :, :, :], AX.X, ALU.add))
                        chain.link(nc.vector.tensor_scalar(xin[:, :, D:20], xin[:, :, D:20],
                                                           3.0 ** -0.5, None, ALU.mult))
                        x = xin[:, :, :]
                    for j in range(4):
                        dve.wait_ge(weights_made, c * 4 + j + 1)
                        nc.vector.tensor_mul(
                            prod[:, j % 2, :, :, :],
                            weights[:, 2 * (j % 2):2 * (j % 2) + 2, 0:320]
                            .rearrange("p t (i o) -> p t o i", o=no),
                            x[:, 2 * j:2 * j + 2, :].unsqueeze(2).to_broadcast([P, 2, no, ni]))\
                            .then_inc(weights_used, 1)
                        if j == 0 and (not isinstance(c, int) or c > 0):
                            add_up(c - 1, (slot - 1) % RING)
                        dve.wait_ge(weights_used, c * 4 + j + 1)
                        dst = mixed if kind == "tensor0" else values[:, slot % 2, :, :]
                        ins = nc.vector.tensor_reduce(dst[:, 2 * j:2 * j + 2, :],
                                                      prod[:, j % 2, :, :, :], AX.X, ALU.add)
                    if kind == "tensor1":
                        ins.then_inc(values_made, 1)
                    else:
                        chain.link(ins)
                        chain.link(nc.vector.tensor_copy(values[:, slot % 2, :, 0:D], mixed[:, :, 0:D]))
                        nc.vector.tensor_tensor(
                            values[:, slot % 2, :, D:28].rearrange("p g (j c) -> p g j c", c=3),
                            mixed[:, :, D:20].unsqueeze(3).to_broadcast([P, G, 4, 3]),
                            sh.unsqueeze(2).to_broadcast([P, G, 4, 3]), ALU.mult).then_inc(values_made, 1)
                    chain.end()

                s_chain = Chain(dve, sheaf_chain, per=17) if sheaf else None

                def sheaf_math(c, slot):
                    par = slot % 2
                    s_chain.turn(c)
                    link = s_chain.link
                    dve.wait_ge(refl_made, c + 1)
                    refl = out_ps[:, par, G * D:3 * G * D].rearrange("p (g a i) -> p g a i", a=2, i=D)
                    b2 = w["b2"][:, :].unsqueeze(1).unsqueeze(1).to_broadcast([P, G, 2, D])
                    vec = values[:, par, :, :, :]
                    link(nc.vector.tensor_add(aba[:, :, 0:2, :], refl, b2))
                    link(nc.vector.tensor_copy(aba[:, :, 2, :], aba[:, :, 0, :]))
                    link(nc.vector.tensor_mul(tmp[:, :, :, :], aba[:, :, 0:2, :], aba[:, :, 0:2, :]))
                    link(nc.vector.tensor_reduce(dot[:, :, :], tmp[:, :, :, :], AX.X, ALU.add))
                    link(nc.vector.tensor_scalar(dot[:, :, :], dot[:, :, :], 1e-24, 0.5, ALU.max, ALU.mult))
                    link(nc.vector.reciprocal(rcp[:, :, 0:2], dot[:, :, :]))
                    link(nc.vector.tensor_copy(rcp[:, :, 2:3], rcp[:, :, 0:1]))
                    nc.vector.tensor_copy(vec[:, :, 0, :], rows[:, slot, :, 0:D])
                    link(nc.vector.tensor_copy(
                        vec[:, :, 1, :], out_ps[:, par, 0:G * D].rearrange("p (g i) -> p g i", i=D)))
                    for n in range(2):
                        r = aba[:, :, n:n + 2, :]
                        link(nc.vector.tensor_mul(tmp[:, :, :, :], r, vec))
                        link(nc.vector.tensor_reduce(dot[:, :, :], tmp[:, :, :, :], AX.X, ALU.add))
                        link(nc.vector.tensor_mul(dot[:, :, :], dot[:, :, :], rcp[:, :, n:n + 2]))
                        link(nc.vector.tensor_mul(tmp[:, :, :, :], r,
                                                  dot[:, :, :].unsqueeze(3).to_broadcast([P, G, 2, D])))
                        ins = nc.vector.tensor_sub(vec, vec, tmp[:, :, :, :])
                        if n == 0:
                            link(ins)
                    ins.then_inc(values_made, 1)
                    s_chain.end()

                def sheaf_body(c, slot, turn):
                    one_hots(c, slot, turn)
                    if not isinstance(c, int) or c > 0:
                        if not isinstance(c, int) or c > 2:
                            dve.wait_ge(msg_out[(slot - 1) % 2], turn_of(turn, slot) * 16)
                        sheaf_math(c - 1, (slot - 1) % RING)
                    if not isinstance(c, int) or c > 1:
                        add_up(c - 2, (slot - 2) % RING)

                def turn_of(turn, slot):
                    return turn * 2 + (slot - 1) // 2

                if tensor:
                    run_chunks(dve, C, RING, tensor_body)
                    add_up(C - 1, (C - 1) % RING)
                elif sheaf:
                    run_chunks(dve, C, RING, sheaf_body)
                    dve.wait_ge(msg_out[(C - 1) % 2], (C - 1) // 2 * 16)
                    sheaf_math(C - 1, (C - 1) % RING)
                    add_up(C - 2, (C - 2) % RING)
                    add_up(C - 1, (C - 1) % RING)
                else:
                    run_chunks(dve, C, RING, simple_body)
                    add_up(C - 1, (C - 1) % RING)


def node_linear(nc, k, tag, terms, outs, width):
    with ExitStack() as ctx:
        sem = ctx.enter_context(phase_semaphores(nc, tag))

        turned = [ctx.enter_context(nc.psum_tensor(f"{tag}_turned{n}", [P, P], F32)) for n in range(len(terms))]
        lhs = [ctx.enter_context(nc.sbuf_tensor(f"{tag}_lhs{n}", [P, P], F32)) for n in range(len(terms))]
        staged = [ctx.enter_context(nc.sbuf_tensor(f"{tag}_staged{n}", [P, P], F32)) for n in range(len(terms))]
        sums = ctx.enter_context(nc.psum_tensor(f"{tag}_sums", [P, 512], F32))
        rows_staged = sem("rows_staged")
        ones_set, rows_turned, lhs_made, product_made, product_out = (
            sem("ones_set"), sem("rows_turned"), sem("lhs_made"), sem("product_made"), sem("product_out"))
        with nc.Block() as block:
            @block.gpsimd
            def _(pool):
                def body(i):
                    wait_past(pool, rows_turned, i)
                    for n, (rows, stride, first, count, _) in enumerate(terms):
                        ins = nc.gpsimd.tensor_copy(staged[n][:, 0:count],
                                                    rows[:, bass.ds(i * stride + first, count)])
                    ins.then_inc(rows_staged, 1)
                body(0)
                with pool.Fori(1, NB) as i:
                    body(i)

            @block.tensor
            def _(pe):
                def body(i):
                    pe.wait_ge(rows_staged, i + 1)
                    for n, (_, _, _, count, _) in enumerate(terms):
                        ins = nc.tensor.transpose(turned[n][0:count, :], staged[n][:, 0:count],
                                                  k["ident"][:, :])
                    ins.then_inc(rows_turned, 1)
                    pe.wait_ge(lhs_made, i + 1)
                    wait_past(pe, product_out, i)
                    for n, (_, _, _, _, wt) in enumerate(terms):
                        ins = nc.tensor.matmul(sums[:, 0:width], lhs[n][0:wt.shape[0], :], wt,
                                               start=n == 0, stop=n == len(terms) - 1)
                    ins.then_inc(product_made, 1)
                body(0)
                with pe.Fori(1, NB) as i:
                    body(i)

            @block.vector
            def _(dve):
                for t in lhs:
                    nc.vector.memset(t[:, :], 1.0).then_inc(ones_set, 1)
                dve.wait_ge(ones_set, len(lhs))

                def body(i):
                    dve.wait_ge(rows_turned, i + 1)
                    wait_past(dve, product_made, i)
                    for n, (_, _, _, count, _) in enumerate(terms):
                        ins = nc.vector.tensor_copy(lhs[n][0:count, :], turned[n][0:count, :])
                    ins.then_inc(lhs_made, 1)
                body(0)
                with dve.Fori(1, NB) as i:
                    body(i)

            @block.scalar
            def _(act):
                def body(i):
                    act.wait_ge(product_made, i + 1)
                    for tile, stride, first, src, n in outs:
                        ins = nc.scalar.copy(tile[:, bass.ds(i * stride + first, n)], sums[:, src:src + n])
                    ins.then_inc(product_out, 1)
                body(0)
                with act.Fori(1, NB) as i:
                    body(i)
                act.wait_ge(product_out, NB)


def node_steps(nc, k, tag, steps, store=None):
    with ExitStack() as ctx:
        sem = ctx.enter_context(phase_semaphores(nc, tag))

        part = ctx.enter_context(nc.psum_tensor(f"{tag}_part", [P, 64], F32))
        order, root_ready, root_done, part_ready, part_done, rows_ready, rows_out = (
            sem("order"), sem("root_ready"), sem("root_done"), sem("part_ready"), sem("part_done"),
            sem("rows_ready"), sem("rows_out"))
        roots, totals = [], []
        with nc.Block() as block:
            @block.vector
            def _(dve):
                chain = Chain(dve, order)

                class V:
                    link = staticmethod(chain.link)

                    @staticmethod
                    def root(ap):
                        roots.append(ap)
                        dve.sem_inc(root_ready, 1)
                        dve.wait_ge(root_done, len(roots))

                    @staticmethod
                    def total(ap, n):
                        totals.append((ap, n))
                        dve.sem_inc(part_ready, 1)
                        dve.wait_ge(part_done, len(totals))
                        return part[:, 0:n]
                steps(V)
                dve.sem_inc(rows_ready, 1)

            @block.scalar
            def _(act):
                for n, ap in enumerate(roots):
                    act.wait_ge(root_ready, n + 1)
                    nc.scalar.activation(ap, ap, ACT.Sqrt).then_inc(root_done, 1)

            @block.tensor
            def _(pe):
                for n, (ap, width) in enumerate(totals):
                    pe.wait_ge(part_ready, n + 1)
                    nc.tensor.matmul(part[:, 0:width], k["ones"][:, :], ap, start=True, stop=True)\
                        .then_inc(part_done, 1)

            @block.sync
            def _(sp):
                if store is not None:
                    sp.wait_ge(rows_ready, 1)
                    for n, (dst, src) in enumerate(store):
                        sp.dma_start(dst, src).then_inc(rows_out, 16)
                    sp.wait_ge(rows_out, 16 * len(store))


def layers(nc, x, src, dst, ea3, ea48, ea8, W1, b1, W2, b2, f0w1, f0b1, f0w2, f0b2, f1w1, f1b1, f1w2, f1b2,
           gs0, bs0, gv0, gs1, bs1, ew, eb, rw, rb, gam, bet, pw, pb, W, b, out):
    def dram(name, shape, dt=F32):
        return nc.dram_tensor(name, shape, dt, kind="Internal").ap()

    rec_d, rec_s = dram("rec_by_dst", (T * P, RD)), dram("rec_by_src", (T * P, RS))
    msg = dram("src_messages", (T * P, D))
    blk_dram = {"s": dram("blocks_by_src", (T,), I32), "d": dram("blocks_by_dst", (T,), I32)}
    table0 = dram("table_sheaf", (NB * P, D + P))
    tables = [dram(f"table{n}", (NB * P, D)) for n in range(5)]
    table_v = dram("table_vectors", (NB * P, 28))
    nl = ew.shape[0]
    with ExitStack() as ctx:
        def sb(name, shape, dt=F32):
            return ctx.enter_context(nc.sbuf_tensor(name, shape, dt))

        k = make_consts(nc, ctx)
        blk = {q: sb(f"blk_{q}", [1, T], I32) for q in "sd"}
        deg = {q: sb(f"deg_{q}", [P, NB]) for q in "sd"}
        wpq, w2t, b2b = sb("wpq", [D + 1, 4 * 64]), sb("w2t", [P, 2 * D]), sb("b2b", [P, D])
        tw1 = [sb(f"tw1_{n}", [48, 48]) for n in range(2)]
        tb1 = [sb(f"tb1_{n}", [48, 1]) for n in range(2)]
        tw2 = [sb(f"tw2_{n}", [49, 320]) for n in range(2)]
        gains = {n: sb(f"gain_{n}", [P, a.shape[-1]]) for n, a in
                 (("gs0", gs0), ("bs0", bs0), ("gv0", gv0), ("gs1", gs1), ("bs1", bs1), ("b", b))}
        gamb = [sb(f"gam{n}", [P, D]) for n in range(nl - 1)]
        betb = [sb(f"bet{n}", [P, D]) for n in range(nl - 1)]
        edge_w = [sb(f"edge_w{n}", [P, D]) for n in range(nl)]
        edge_b = [sb(f"edge_b{n}", [D, D]) for n in range(nl)]
        root_w = [sb(f"root_w{n}", [D + 1, D]) for n in range(nl)]
        pred_w, last_w = sb("pred_w", [D + 1, D]), sb("last_w", [D, D])
        X, H, S = sb("X", [P, NB * D]), sb("H", [P, NB * D]), sb("S", [P, NB * 28])
        st = [sb(f"st{n}", [P, NB]) for n in range(4)]
        dis = sb("dis", [P, NB])
        s_w, s_wz = ctx.enter_context(nc.semaphore("weights_in")), ctx.enter_context(nc.semaphore("w_zero"))

        def v3(t, f=D, first=0, count=None):
            return t[:, 0:NB * f].rearrange("p (b f) -> p b f", f=f)[:, :, first:first + (count or f)]

        def rows_of(ap):
            return ap.rearrange("(b p) f -> p b f", p=P)

        def row1(ap):
            return ap.rearrange("(a n) -> a n", a=1)

        def gathers(name):
            return [ctx.enter_context(nc.semaphore(f"{name}_rows_in{r}")) for r in range(RING)]

        with nc.Block() as block:
            @block.vector
            def _(dve):
                nc.vector.memset(w2t[:, :], 0.0).then_inc(s_wz, 1)
                nc.vector.memset(wpq[:, :], 0.0).then_inc(s_wz, 1)
                nc.vector.memset(X[:, :], 0.0).then_inc(s_wz, 1)

            @block.sync
            def _(sp):
                sp.wait_ge(s_wz, 3)
                loads = []
                with nc.allow_non_contiguous_dma(reason="small weights, turned"):
                    for at, a in ((0, 0), (64, D), (128, D), (192, 0)):
                        loads.append((wpq[0:D, at:at + 64], W1[:, a:a + D].rearrange("h f -> f h")))
                    for at in (0, 64):
                        loads.append((wpq[D:D + 1, at:at + 64], row1(b1)))
                    for n in range(2):
                        loads.append((w2t[n * 64:(n + 1) * 64, n * D:(n + 1) * D], W2.rearrange("d h -> h d")))
                    loads.append((b2b[:, :], row1(b2).to_broadcast([P, D])))
                    for n, (a1, c1, a2, c2) in enumerate(((f0w1, f0b1, f0w2, f0b2), (f1w1, f1b1, f1w2, f1b2))):
                        loads.append((tw1[n][:, :], a1))
                        loads.append((tb1[n][:, :], c1.rearrange("(n a) -> n a", a=1)))
                        for rows, m in ((slice(0, 48), a2), (slice(48, 49), row1(c2))):
                            if n == 0:
                                t = tw2[0][rows, :].rearrange("k (i o) -> k i o", o=20)
                                loads.append((t[:, :, 0:D], m[:, 0:256].rearrange("k (i o) -> k i o", o=D)))
                                loads.append((t[:, :, D:20], m[:, 256:320].rearrange("k (i o) -> k i o", o=4)))
                            else:
                                loads.append((tw2[1][rows, :], m))
                    for n, a in (("gs0", gs0), ("bs0", bs0), ("gv0", gv0), ("gs1", gs1), ("bs1", bs1), ("b", b)):
                        loads.append((gains[n][:, :], row1(a).to_broadcast([P, a.shape[0]])))
                    for n in range(nl - 1):
                        loads.append((gamb[n][:, :], gam[n:n + 1, :].to_broadcast([P, D])))
                        loads.append((betb[n][:, :], bet[n:n + 1, :].to_broadcast([P, D])))
                    for n in range(nl):
                        loads.append((edge_w[n][:, :], ew[n].rearrange("k (i o) -> (k i) o", o=D)))
                        loads.append((edge_b[n][:, :], eb[n].rearrange("(i o) -> i o", o=D)))
                        loads.append((root_w[n][0:D, :], rw[n]))
                        loads.append((root_w[n][D:D + 1, :], rb[n:n + 1, :]))
                    loads.append((pred_w[0:D, :], pw))
                    loads.append((pred_w[D:D + 1, :], row1(pb)))
                    loads.append((last_w[:, :], W))
                    loads.append((v3(X)[:, 0:NB - 1, :], x[0:(NB - 1) * P, :].rearrange("(b p) f -> p b f", p=P)))
                    loads.append((v3(X)[0:LAST, NB - 1, :], x[(NB - 1) * P:N, :]))
                    for dst_ap, src_ap in loads:
                        sp.dma_start(dst_ap, src_ap).then_inc(s_w, 16)
                sp.wait_ge(s_w, 16 * len(loads))

        sort_edges(nc, k, src, dst, ea3, ea48, ea8, rec_d, rec_s, blk_dram, blk, deg,
                   [ctx.enter_context(nc.semaphore(f"sorted_out{h}")) for h in range(2)])

        def bc(stat):
            return stat[:, :].unsqueeze(2).to_broadcast([P, NB, D])

        def feat(row, f=D):
            return row.unsqueeze(1).to_broadcast([P, NB, f])

        def norm_rows(v, t):
            vec = nc.vector
            v.link(vec.tensor_reduce(st[0][:, :], v3(t), AX.X, ALU.add))
            v.link(vec.tensor_scalar(st[0][:, :], st[0][:, :], 1.0 / D, None, ALU.mult))
            v.link(vec.tensor_sub(v3(t), v3(t), bc(st[0])))
            v.link(vec.tensor_mul(v3(S), v3(t), v3(t)))
            v.link(vec.tensor_reduce(st[1][:, :], v3(S), AX.X, ALU.add))
            v.link(vec.tensor_scalar(st[1][:, :], st[1][:, :], 1.0 / D, EPS, ALU.mult, ALU.add))
            v.root(st[1][:, :])
            v.link(vec.reciprocal(st[1][:, :], st[1][:, :]))
            v.link(vec.tensor_mul(v3(t), v3(t), bc(st[1])))

        def norm_batch(v, t, gain, shift):
            vec = nc.vector
            sm = st[2]
            pad = t[:, NB - 1, :]
            mask = k["in_last"][:, 0:1]
            v.link(vec.tensor_scalar(pad, pad, mask, None, ALU.mult))
            v.link(vec.tensor_reduce(sm[:, 0:D], t.rearrange("p b f -> p f b"), AX.X, ALU.add))
            v.link(vec.tensor_scalar(sm[:, D:2 * D], v.total(sm[:, 0:D], D), 1.0 / N, None, ALU.mult))
            v.link(vec.tensor_sub(t, t, feat(sm[:, D:2 * D])))
            v.link(vec.tensor_scalar(pad, pad, mask, None, ALU.mult))
            v.link(vec.tensor_mul(v3(S), t, t))
            v.link(vec.tensor_reduce(sm[:, 0:D], v3(S).rearrange("p b f -> p f b"), AX.X, ALU.add))
            v.link(vec.tensor_scalar(sm[:, D:2 * D], v.total(sm[:, 0:D], D), 1.0 / N, EPS, ALU.mult, ALU.add))
            v.root(sm[:, D:2 * D])
            v.link(vec.reciprocal(sm[:, D:2 * D], sm[:, D:2 * D]))
            v.link(vec.tensor_mul(sm[:, D:2 * D], sm[:, D:2 * D], gain))
            v.link(vec.tensor_mul(t, t, feat(sm[:, D:2 * D])))
            v.link(vec.tensor_add(t, t, feat(shift)))

        def scale0(v):
            vec = nc.vector
            v.link(vec.tensor_add(dis[:, :], deg["s"][:, :], deg["d"][:, :]))
            v.link(vec.tensor_scalar(dis[:, :], dis[:, :], 1e-5, None, ALU.max))
            v.root(dis[:, :])
            v.link(vec.reciprocal(dis[:, :], dis[:, :]))
            v.link(vec.tensor_mul(v3(H), v3(X), bc(dis)))

        node_steps(nc, k, "scale0", scale0, [(rows_of(table0)[:, :, 0:D], v3(H))])
        with ExitStack() as l0:
            own = l0.enter_context(nc.sbuf_tensor("own_pq", [P, NB * P], F32))
            acc_d = l0.enter_context(nc.sbuf_tensor("acc_d", [P, NB * D], F32))
            acc_s = l0.enter_context(nc.sbuf_tensor("acc_s", [P, NB * D], F32))
            with ExitStack() as l00:
                pq = l00.enter_context(nc.sbuf_tensor("pq", [P, NB * P], F32))
                node_linear(nc, k, "pq", [(X, D, 0, D, wpq[:, :])], [(pq, P, 0, 0, P), (own, P, 0, P, P)], 2 * P)
                node_steps(nc, k, "pq_out", lambda v: None, [(rows_of(table0)[:, :, D:D + P], v3(pq, P))])
            edge_pass(nc, k, "sheaf", "sheaf", rec_d, RD, table0, D + P, blk["d"], acc_d, D,
                      {"y": H, "own": own, "w2": w2t, "b2": b2b, "msg": msg}, gathers("sheaf"))
            edge_pass(nc, k, "back", "row", rec_s, RS, msg, D, blk["s"], acc_s, D, {}, gathers("back"))

            def end0(v):
                vec = nc.vector
                v.link(vec.tensor_add(acc_d[:, :], acc_d[:, :], acc_s[:, :]))
                v.link(vec.tensor_mul(v3(acc_d), v3(acc_d), bc(dis)))
                v.link(vec.tensor_add(acc_d[:, :], acc_d[:, :], X[:, :]))
                v.link(vec.scalar_tensor_tensor(X[:, :], acc_d[:, :], 0.0, X[:, :], ALU.max, ALU.add))
                norm_rows(v, X)

            node_steps(nc, k, "end0", end0, [(rows_of(tables[0]), v3(X))])

        with ExitStack() as l1:
            acc = l1.enter_context(nc.sbuf_tensor("acc_l1", [P, NB * 28], F32))
            acc1 = l1.enter_context(nc.sbuf_tensor("acc_l1b", [P, NB * D], F32))
            edge_pass(nc, k, "conv0", "tensor0", rec_s, RS, tables[0], D, blk["s"], acc, 28,
                      {"w1": tw1[0], "b1": tb1[0], "w2": tw2[0]}, gathers("conv0"))

            def mid1(v):
                vec = nc.vector
                v.link(vec.tensor_scalar(dis[:, :], deg["s"][:, :], 1.0, None, ALU.max))
                v.link(vec.reciprocal(dis[:, :], dis[:, :]))
                v.link(vec.tensor_scalar(st[3][:, :], dis[:, :], D ** -0.5, None, ALU.mult))
                v.link(vec.tensor_mul(v3(acc, 28), v3(acc, 28),
                                      st[3][:, :].unsqueeze(2).to_broadcast([P, NB, 28])))
                norm_batch(v, v3(acc, 28, 0, D), gains["gs0"][:, :], gains["bs0"][:, :])
                vectors = v3(acc, 28, D, 12)
                v.link(vec.tensor_mul(v3(S, 12), vectors, vectors))
                v.link(vec.tensor_reduce(st[2][:, 0:12], v3(S, 12).rearrange("p b f -> p f b"), AX.X, ALU.add))
                total = v.total(st[2][:, 0:12], 12)
                v.link(vec.tensor_reduce(st[2][:, 16:20], total.rearrange("p (j c) -> p j c", c=3), AX.X, ALU.add))
                v.link(vec.tensor_scalar(st[2][:, 16:20], st[2][:, 16:20], 1.0 / (3 * N), EPS, ALU.mult, ALU.add))
                v.root(st[2][:, 16:20])
                v.link(vec.reciprocal(st[2][:, 16:20], st[2][:, 16:20]))
                v.link(vec.tensor_mul(st[2][:, 16:20], st[2][:, 16:20], gains["gv0"][:, :]))
                v.link(vec.tensor_copy(st[2][:, 32:44].rearrange("p (j c) -> p j c", c=3),
                                       st[2][:, 16:20].unsqueeze(2).to_broadcast([P, 4, 3])))
                v.link(vec.tensor_mul(vectors, vectors, feat(st[2][:, 32:44], 12)))

            node_steps(nc, k, "mid1", mid1, [(rows_of(table_v), v3(acc, 28))])
            edge_pass(nc, k, "conv1", "tensor1", rec_s, RS, table_v, 28, blk["s"], acc1, D,
                      {"w1": tw1[1], "b1": tb1[1], "w2": tw2[1]}, gathers("conv1"))

            def end1(v):
                vec = nc.vector
                v.link(vec.tensor_scalar(st[3][:, :], dis[:, :], 20.0 ** -0.5, None, ALU.mult))
                v.link(vec.tensor_mul(v3(acc1), v3(acc1), bc(st[3])))
                norm_batch(v, v3(acc1), gains["gs1"][:, :], gains["bs1"][:, :])
                v.link(vec.tensor_add(X[:, :], X[:, :], acc1[:, :]))
                norm_rows(v, X)
                v.link(vec.tensor_copy(H[:, :], X[:, :]))

            node_steps(nc, k, "end1", end1, [(rows_of(tables[1]), v3(X))])

        with ExitStack() as l2:
            acc = l2.enter_context(nc.sbuf_tensor("acc_l2", [P, NB * 144], F32))
            H2 = l2.enter_context(nc.sbuf_tensor("H2", [P, NB * D], F32))
            for n in range(nl):
                edge_pass(nc, k, f"nn{n}", "outer", rec_d, RD, tables[1 + n], D, blk["d"], acc, 144, {},
                          gathers(f"nn{n}"))
                node_linear(nc, k, f"nnw{n}", [(acc, 144, 0, P, edge_w[n][:, :]),
                                               (acc, 144, P, D, edge_b[n][:, :]),
                                               (H, D, 0, D, root_w[n][:, :])], [(H2, D, 0, 0, D)], D)
                last = n == nl - 1

                def end2(v):
                    if not last:
                        norm_batch(v, v3(H2), gamb[n][:, :], betb[n][:, :])
                    v.link(nc.vector.tensor_scalar(H[:, :], H2[:, :], 0.0, None, ALU.max))

                node_steps(nc, k, f"end2_{n}", end2, None if last else [(rows_of(tables[2 + n]), v3(H))])
            node_linear(nc, k, "pred", [(H, D, 0, D, pred_w[:, :])], [(H2, D, 0, 0, D)], D)

            def end3(v):
                v.link(nc.vector.tensor_add(X[:, :], X[:, :], H2[:, :]))
                norm_rows(v, X)

            node_steps(nc, k, "end3", end3)

        node_linear(nc, k, "last", [(X, D, 0, D, last_w[:, :])], [(H, D, 0, 0, D)], D)

        def scale3(v):
            vec = nc.vector
            v.link(vec.tensor_scalar(dis[:, :], deg["d"][:, :], 1.0, None, ALU.add))
            v.root(dis[:, :])
            v.link(vec.reciprocal(dis[:, :], dis[:, :]))
            v.link(vec.tensor_mul(v3(H), v3(H), bc(dis)))

        node_steps(nc, k, "scale3", scale3, [(rows_of(tables[4]), v3(H))])
        with ExitStack() as l3:
            acc = l3.enter_context(nc.sbuf_tensor("acc_l3", [P, NB * D], F32))
            edge_pass(nc, k, "gcn", "plain", rec_d, RD, tables[4], D, blk["d"], acc, D, {}, gathers("gcn"))

            def end4(v):
                vec = nc.vector
                v.link(vec.tensor_add(acc[:, :], acc[:, :], H[:, :]))
                v.link(vec.tensor_mul(v3(acc), v3(acc), bc(dis)))
                v.link(vec.tensor_add(v3(acc), v3(acc), feat(gains["b"][:, :])))
                v.link(vec.tensor_add(X[:, :], X[:, :], acc[:, :]))
                norm_rows(v, X)

            node_steps(nc, k, "end4", end4,
                       [(out[0:(NB - 1) * P, :].rearrange("(b p) f -> p b f", p=P), v3(X)[:, 0:NB - 1, :]),
                        (out[(NB - 1) * P:N, :], v3(X)[0:LAST, NB - 1, :])])


_INS = ["x", "src", "dst", "edge_attr_3", "edge_attr_48", "edge_attr_8", "L0_gnn_W1", "L0_gnn_b1", "L0_gnn_W2",
        "L0_gnn_b2", "L1_gnn_fc0_w1", "L1_gnn_fc0_b1", "L1_gnn_fc0_w2", "L1_gnn_fc0_b2", "L1_gnn_fc1_w1",
        "L1_gnn_fc1_b1", "L1_gnn_fc1_w2", "L1_gnn_fc1_b2", "L1_gnn_bn0_gs", "L1_gnn_bn0_bs", "L1_gnn_bn0_gv",
        "L1_gnn_bn1_gs", "L1_gnn_bn1_bs", "L2_gnn_edge_w", "L2_gnn_edge_b", "L2_gnn_root_w", "L2_gnn_root_b",
        "L2_gnn_bn_gamma", "L2_gnn_bn_beta", "L2_gnn_pred_w", "L2_gnn_pred_b", "L3_gnn_W", "L3_gnn_b"]


def kernel(**inputs):
    import numpy as _np
    import concourse.bacc as _bacc
    from concourse import mybir as _mybir
    from concourse.bass_utils import run_bass_kernel_spmd as _run

    nc = _bacc.Bacc("TRN2", target_bir_lowering=False, num_devices=1)
    arrays, args = {}, []
    for name in _INS:
        a = _np.ascontiguousarray(inputs[name])
        arrays[f"in_{name}"] = a
        args.append(nc.dram_tensor(f"in_{name}", a.shape, _mybir.dt.from_np(a.dtype), kind="ExternalInput").ap())
    args.append(nc.dram_tensor("out_rows", (N, D), F32, kind="ExternalOutput").ap())
    layers(nc, *args)
    return _run(nc, [arrays], core_ids=[0]).results[0]["out_rows"]
```
